# Optimizing a Trainium2 kernel written in Bass

```python
import numpy as np
import jax
import jax.numpy as jnp

def _softmax(x, axis=-1):
    return jax.nn.softmax(x, axis=axis)

def _gelu(x):
    return jax.nn.gelu(x, approximate=True)

def _silu(x):
    return jax.nn.silu(x)

def _sigmoid(x):
    return jax.nn.sigmoid(x)

def _layernorm(x, axis=-1, eps=1e-05):
    m = jnp.mean(x, axis=axis, keepdims=True)
    v = jnp.var(x, axis=axis, keepdims=True)
    return (x - m) / jnp.sqrt(v + eps)

def _scatter_add(tgt, idx, src, axis=0):
    return tgt.at[idx].add(src)

def _segment_sum(src, seg, n):
    return jax.ops.segment_sum(src, seg, n)
kernel_name = 'mk_rec_standalone_d1_rec_r8_9440a1'

def setup_inputs(seed: int=0):
    np.random.seed(seed)
    _w = jnp.asarray

    def _rec_inputs():
        import jax
        import jax.numpy as jnp
        _rk = jax.random.key(seed)
        r_dense_x = 8.7408e-05 + 1.0001 * jax.random.normal(jax.random.fold_in(_rk, 1), (2048, 13), jnp.float32)
        r_sparse_x = jnp.stack([jax.random.randint(jax.random.fold_in(jax.random.fold_in(_rk, 2), 0), (2048,), 2, 12500, jnp.int32), jax.random.randint(jax.random.fold_in(jax.random.fold_in(_rk, 2), 1), (2048,), 1, 99999, jnp.int32), jax.random.randint(jax.random.fold_in(jax.random.fold_in(_rk, 2), 2), (2048,), 0, 12500, jnp.int32), jax.random.randint(jax.random.fold_in(jax.random.fold_in(_rk, 2), 3), (2048,), 0, 12500, jnp.int32), jax.random.randint(jax.random.fold_in(jax.random.fold_in(_rk, 2), 4), (2048,), 10, 99997, jnp.int32), jax.random.randint(jax.random.fold_in(jax.random.fold_in(_rk, 2), 5), (2048,), 0, 99993, jnp.int32), jax.random.randint(jax.random.fold_in(jax.random.fold_in(_rk, 2), 6), (2048,), 2, 99999, jnp.int32), jax.random.randint(jax.random.fold_in(jax.random.fold_in(_rk, 2), 7), (2048,), 1, 99995, jnp.int32), jax.random.randint(jax.random.fold_in(jax.random.fold_in(_rk, 2), 8), (2048,), 0, 12500, jnp.int32), jax.random.randint(jax.random.fold_in(jax.random.fold_in(_rk, 2), 9), (2048,), 2, 99999, jnp.int32), jax.random.randint(jax.random.fold_in(jax.random.fold_in(_rk, 2), 10), (2048,), 0, 99999, jnp.int32), jax.random.randint(jax.random.fold_in(jax.random.fold_in(_rk, 2), 11), (2048,), 6, 99999, jnp.int32), jax.random.randint(jax.random.fold_in(jax.random.fold_in(_rk, 2), 12), (2048,), 0, 99999, jnp.int32), jax.random.randint(jax.random.fold_in(jax.random.fold_in(_rk, 2), 13), (2048,), 3, 99996, jnp.int32), jax.random.randint(jax.random.fold_in(jax.random.fold_in(_rk, 2), 14), (2048,), 0, 99999, jnp.int32), jax.random.randint(jax.random.fold_in(jax.random.fold_in(_rk, 2), 15), (2048,), 3, 99997, jnp.int32), jax.random.randint(jax.random.fold_in(jax.random.fold_in(_rk, 2), 16), (2048,), 0, 99999, jnp.int32), jax.random.randint(jax.random.fold_in(jax.random.fold_in(_rk, 2), 17), (2048,), 0, 99998, jnp.int32), jax.random.randint(jax.random.fold_in(jax.random.fold_in(_rk, 2), 18), (2048,), 10, 99997, jnp.int32), jax.random.randint(jax.random.fold_in(jax.random.fold_in(_rk, 2), 19), (2048,), 0, 99999, jnp.int32), jax.random.randint(jax.random.fold_in(jax.random.fold_in(_rk, 2), 20), (2048,), 0, 12500, jnp.int32), jax.random.randint(jax.random.fold_in(jax.random.fold_in(_rk, 2), 21), (2048,), 1, 12500, jnp.int32), jax.random.randint(jax.random.fold_in(jax.random.fold_in(_rk, 2), 22), (2048,), 1, 99997, jnp.int32), jax.random.randint(jax.random.fold_in(jax.random.fold_in(_rk, 2), 23), (2048,), 2, 12500, jnp.int32), jax.random.randint(jax.random.fold_in(jax.random.fold_in(_rk, 2), 24), (2048,), 1, 12500, jnp.int32), jax.random.randint(jax.random.fold_in(jax.random.fold_in(_rk, 2), 25), (2048,), 2, 99995, jnp.int32)], axis=1)
        return (r_dense_x, r_sparse_x)
    r_dense_x, r_sparse_x = _rec_inputs()

    def _L0_rec_setup():
        import jax, jax.numpy as jnp
        import numpy as np
        B = 4096
        NUM_SPARSE = 26
        VOCAB = 12500
        EMB = 128
        DENSE_IN = 13
        N_FIELDS = NUM_SPARSE + 1
        INTER_DIM = N_FIELDS * (N_FIELDS - 1) // 2
        TOP_IN = EMB + INTER_DIM
        key = jax.random.key(seed)
        ks = jax.random.split(key, 12)
        inp = {'dense_x': jax.random.normal(ks[0], (B, DENSE_IN), dtype=jnp.float32), 'sparse_x': jax.random.randint(ks[1], (B, NUM_SPARSE), 0, VOCAB, dtype=jnp.int64), 'emb_tables': jax.random.normal(ks[2], (NUM_SPARSE, VOCAB, EMB), dtype=jnp.float32) * 0.02, 'bw1': jax.random.normal(ks[3], (DENSE_IN, 256), dtype=jnp.float32) * 0.1, 'bb1': jnp.zeros((256,), dtype=jnp.float32), 'bw2': jax.random.normal(ks[4], (256, EMB), dtype=jnp.float32) * 0.05, 'bb2': jnp.zeros((EMB,), dtype=jnp.float32), 'tw1': jax.random.normal(ks[5], (TOP_IN, 128), dtype=jnp.float32) * 0.05, 'tb1': jnp.zeros((128,), dtype=jnp.float32), 'tw2': jax.random.normal(ks[6], (128, 64), dtype=jnp.float32) * 0.1, 'tb2': jnp.zeros((64,), dtype=jnp.float32), 'tw3': jax.random.normal(ks[7], (64, 1), dtype=jnp.float32) * 0.1, 'tb3': jnp.zeros((1,), dtype=jnp.float32)}
        return inp
    _L0_rec_all = _L0_rec_setup()
    _L0_rec_in = {k: v for k, v in _L0_rec_all.items() if k in ('emb_tables', 'bw1', 'bb1', 'bw2', 'bb2', 'tw1', 'tb1', 'tw2', 'tb2', 'tw3', 'tb3')}
    del _L0_rec_all
    return {'r_dense_x': r_dense_x, 'r_sparse_x': r_sparse_x, 'L0_rec_emb_tables': _L0_rec_in['emb_tables'], 'L0_rec_bw1': _L0_rec_in['bw1'], 'L0_rec_bb1': _L0_rec_in['bb1'], 'L0_rec_bw2': _L0_rec_in['bw2'], 'L0_rec_bb2': _L0_rec_in['bb2'], 'L0_rec_tw1': _L0_rec_in['tw1'], 'L0_rec_tb1': _L0_rec_in['tb1'], 'L0_rec_tw2': _L0_rec_in['tw2'], 'L0_rec_tb2': _L0_rec_in['tb2'], 'L0_rec_tw3': _L0_rec_in['tw3'], 'L0_rec_tb3': _L0_rec_in['tb3']}

def reference(r_dense_x, r_sparse_x, L0_rec_emb_tables, L0_rec_bw1, L0_rec_bb1, L0_rec_bw2, L0_rec_bb2, L0_rec_tw1, L0_rec_tb1, L0_rec_tw2, L0_rec_tb2, L0_rec_tw3, L0_rec_tb3):
    import jax
    import jax.numpy as jnp

    def _L0_rec_ref(dense_x, sparse_x, emb_tables, bw1, bb1, bw2, bb2, tw1, tb1, tw2, tb2, tw3, tb3):
        import jax, jax.numpy as jnp
        import numpy as np
        B = 4096
        NUM_SPARSE = 26
        VOCAB = 12500
        EMB = 128
        DENSE_IN = 13
        N_FIELDS = NUM_SPARSE + 1
        INTER_DIM = N_FIELDS * (N_FIELDS - 1) // 2
        TOP_IN = EMB + INTER_DIM
        h = jax.nn.relu(dense_x @ bw1 + bb1)
        x_bottom = jax.nn.relu(h @ bw2 + bb2)
        field_idx = jnp.arange(NUM_SPARSE)[None, :]
        sparse_embs = emb_tables[field_idx, sparse_x]
        combined = jnp.concatenate([x_bottom[:, None, :], sparse_embs], axis=1)
        interactions = jnp.einsum('bfd,bgd->bfg', combined, combined)
        rows, cols = np.triu_indices(N_FIELDS, k=1)
        x_int = interactions[:, rows, cols]
        x_final = jnp.concatenate([x_bottom, x_int], axis=-1)
        t = jax.nn.relu(x_final @ tw1 + tb1)
        t = jax.nn.relu(t @ tw2 + tb2)
        logits = t @ tw3 + tb3
        return jax.nn.sigmoid(logits)
    y = _L0_rec_ref(r_dense_x, r_sparse_x, L0_rec_emb_tables, L0_rec_bw1, L0_rec_bb1, L0_rec_bw2, L0_rec_bb2, L0_rec_tw1, L0_rec_tb1, L0_rec_tw2, L0_rec_tb2, L0_rec_tw3, L0_rec_tb3)
    return y

_drawn_inputs = setup_inputs


def setup_inputs(seed=0):
    import zlib

    import numpy as np

    out = dict(_drawn_inputs(seed))
    spreads = {'L0_rec_bb1': (0.0, 0.8),
     'L0_rec_bb2': (0.0, 0.8),
     'L0_rec_tb1': (0.0, 1.96),
     'L0_rec_tb2': (0.0, 2.0)}
    factors = {'r_dense_x': 5.76,
     'L0_rec_emb_tables': 8.0,
     'L0_rec_bw1': 4.939,
     'L0_rec_bw2': 4.913,
     'L0_rec_tw1': 4.257,
     'L0_rec_tw2': 3.306}
    for name, (base, spread) in spreads.items():
        noise = np.random.default_rng([zlib.crc32(name.encode()), seed]).standard_normal(out[name].shape)
        drawn = base * np.exp(spread * noise) if base else spread * noise
        out[name] = jnp.asarray(drawn.astype(out[name].dtype))
    for name, factor in factors.items():
        out[name] = (out[name] * factor).astype(out[name].dtype)
    return out
```

```python
from contextlib import ExitStack

import concourse.bass as bass
from concourse import mybir

F32 = mybir.dt.float32
I32 = mybir.dt.int32
U32 = mybir.dt.uint32
ALU = mybir.AluOpType
ACT = mybir.ActivationFunctionType

P = 128
BLOCK = 64
PARTS = 4
QUAD = P // PARTS
T_BANK = 4


def dlrm_kernel(nc, xT, sparse, base, emb, bw1, bb1, bw2, bb2, tw1, tb1, tw2, tb2, tw3, tb3, out):
    DENSE, SAMPLES = xT.shape
    FIELDS, VOCAB, EMB = emb.shape
    HID = bw1.shape[1]
    KH = HID // P
    VECS = FIELDS + 1
    TOP1, TOP2 = tw2.shape
    BLOCKS = SAMPLES // BLOCK
    GATHERS = BLOCK * FIELDS // P
    GROUPS = BLOCK // PARTS
    PAIRS = BLOCKS // 2
    SLICE = 512
    assert EMB == P and TOP1 == P and BLOCK * FIELDS == GATHERS * P and BLOCKS % 2 == 0 and HID == KH * P

    t_chunks = [(k, min(k + T_BANK, GATHERS)) for k in range(0, GATHERS, T_BANK)]
    NT = len(t_chunks)

    def segments(k0, k1):
        row, end, got = P * k0, P * k1, []
        while row < end:
            s, f = divmod(row, FIELDS)
            if f or end - row < FIELDS:
                n, w = 1, min(FIELDS - f, end - row)
            else:
                n, w = (end - row) // FIELDS, FIELDS
            got.append((row - P * k0, s, n, f, w))
            row += n * w
        return got

    groups_per_bank = 512 // (PARTS * FIELDS)
    p_chunks, at = [], 0
    for c, (_, k1) in enumerate(t_chunks):
        whole = P * k1 // FIELDS // PARTS
        if c < len(t_chunks) - 2:
            whole -= (whole - at) % groups_per_bank
        while at < whole:
            p_chunks.append((c, at, min(at + groups_per_bank, whole)))
            at = p_chunks[-1][2]
    assert at == GROUPS and len(p_chunks) == 5 and len(t_chunks) == 4
    NP = len(p_chunks)

    with ExitStack() as ctx:
        def sb(name, shape, dt=F32):
            return ctx.enter_context(nc.sbuf_tensor(name, shape, dt))

        def pb(name, shape):
            return ctx.enter_context(nc.psum_tensor(name, shape, F32))

        def sem(name):
            return ctx.enter_context(nc.semaphore(name))

        ident = sb("ident", [P, P])
        bw1_sb = sb("bw1_sb", [DENSE, HID])
        bw2_sb = sb("bw2_sb", [P, KH, EMB])
        bb1_sb = sb("bb1_sb", [P, KH])
        bb2_sb = sb("bb2_sb", [P, 1])
        tw1_dense = sb("tw1_dense", [P, TOP1])
        tw1_pair = sb("tw1_pair", [P, FIELDS, TOP1])
        tb1_sb = sb("tb1_sb", [P, 1])
        tw2_sb = sb("tw2_sb", [P, TOP2])
        tb2_sb = sb("tb2_sb", [TOP2, 1])
        tw3_sb = sb("tw3_sb", [P, 1])
        tb3_sb = sb("tb3_sb", [1, 1])
        base_sb = sb("base_sb", [P, GATHERS], I32)
        index_sb = sb("index_sb", [P, BLOCKS * GATHERS], I32)
        xT_sb = sb("xT_sb", [DENSE, SAMPLES])
        hidden = sb("hidden", [P, KH, SLICE])
        bottom = sb("bottom", [P, SAMPLES])
        wrap = sb("wrap", [P, 2, GATHERS])
        clipped = sb("clipped", [P, 2, GATHERS])
        rows = sb("rows", [P, 2, GATHERS], U32)
        gathered = sb("gathered", [P, 2, GATHERS, EMB])
        vecs = sb("vecs", [P, 2, BLOCK, QUAD])
        dots = sb("dots", [P, 2, FIELDS, BLOCK])
        top1 = sb("top1", [P, BLOCK])
        top2 = sb("top2", [P, BLOCK])
        prob = sb("prob", [1, SAMPLES])

        t_bank = [pb(f"t_bank{i}", [P, 512]) for i in range(2)]
        p_bank = [pb(f"p_bank{i}", [P, 512]) for i in range(3)]
        top1_bank = pb("top1_bank", [P, 512])
        top2_bank = pb("top2_bank", [P, 512])
        top3_bank = pb("top3_bank", [P, 512])

        s_index0 = sem("s_index0")
        s_index = sem("s_index")
        s_xT = sem("s_xT")
        s_top = sem("s_top")
        s_pair = sem("s_pair")
        s_pair_copy = sem("s_pair_copy")
        s_pair_zero = sem("s_pair_zero")
        s_dots_zero = sem("s_dots_zero")
        s_pad_zero = sem("s_pad_zero")
        s_ident0 = sem("s_ident0")
        s_ident = sem("s_ident")
        s_hid_sum = sem("s_hid_sum")
        s_hid = sem("s_hid")
        s_bot_sum = sem("s_bot_sum")
        s_bottom = sem("s_bottom")
        s_wrap = sem("s_wrap")
        s_clip = sem("s_clip")
        s_rows = sem("s_rows")
        s_gather = [[sem(f"s_gather{p}_{k}") for k in range(GATHERS)] for p in range(2)]
        s_trans = sem("s_trans")
        s_bot_in = sem("s_bot_in")
        s_vecs = sem("s_vecs")
        s_prod = sem("s_prod")
        s_dots = sem("s_dots")
        s_top1_sum = sem("s_top1_sum")
        s_top1 = sem("s_top1")
        s_top2_sum = sem("s_top2_sum")
        s_top2 = sem("s_top2")
        s_top3_sum = sem("s_top3_sum")
        s_prob = sem("s_prob")
        s_out = sem("s_out")

        table = emb.rearrange("f v d -> (f v) d")
        out_row = out.rearrange("(a s) o -> a (s o)", a=1)
        HEAD = 2 * GATHERS

        block = ctx.enter_context(nc.Block())

        @block.sync
        def _(sp):
            sp.dma_start(index_sb[:, 0:HEAD], sparse[:, 0:HEAD]).then_inc(s_index0, 16)
            sp.dma_start(base_sb[:], base).then_inc(s_index0, 16)
            sp.dma_start(xT_sb[:], xT).then_inc(s_xT, 16)
            sp.dma_start(bw1_sb[:], bw1).then_inc(s_xT, 16)
            for k in range(KH):
                sp.dma_start(bb1_sb[:, k:k + 1], bb1[k * P:(k + 1) * P].rearrange("(p a) -> p a", a=1)).then_inc(s_xT, 16)
            sp.dma_start(bw2_sb[:], bw2.rearrange("(k p) n -> p k n", p=P)).then_inc(s_xT, 16)
            sp.dma_start(bb2_sb[:], bb2.rearrange("(p a) -> p a", a=1)).then_inc(s_xT, 16)
            sp.dma_start(index_sb[:, HEAD:], sparse[:, HEAD:]).then_inc(s_index, 16)
            sp.wait_ge(s_pair_zero, 1)
            first = EMB
            for f in range(FIELDS):
                n = FIELDS - f
                sp.dma_start(tw1_pair[f:f + 1, f:FIELDS, :],
                             tw1[first:first + n, :].rearrange("(a g) n -> a g n", a=1)).then_inc(s_pair, 16)
                first += n
            sp.dma_start(tw1_dense[:], tw1[0:EMB, :]).then_inc(s_top, 16)
            sp.dma_start(tb1_sb[:], tb1.rearrange("(p a) -> p a", a=1)).then_inc(s_top, 16)
            sp.dma_start(tw2_sb[:], tw2).then_inc(s_top, 16)
            sp.dma_start(tb2_sb[:], tb2.rearrange("(p a) -> p a", a=1)).then_inc(s_top, 16)
            sp.dma_start(tw3_sb[0:TOP2], tw3).then_inc(s_top, 16)
            sp.dma_start(tb3_sb[:], tb3.rearrange("(p a) -> p a", a=1)).then_inc(s_top, 16)
            sp.wait_ge(s_pair, 16 * FIELDS)
            for q in range(1, PARTS):
                sp.dma_start(tw1_pair[QUAD * q:QUAD * q + FIELDS], tw1_pair[0:FIELDS]).then_inc(s_pair_copy, 16)
            most = SAMPLES - BLOCK
            sp.wait_ge(s_prob, BLOCKS - 1)
            sp.dma_start(out_row[:, 0:most], prob[:, 0:most]).then_inc(s_out, 16)
            sp.wait_ge(s_prob, BLOCKS)
            sp.dma_start(out_row[:, most:], prob[:, most:]).then_inc(s_out, 16)
            sp.wait_ge(s_out, 32)

        @block.gpsimd
        def _(pool):
            nc.gpsimd.memset(ident[:], 0.0).then_inc(s_ident0, 1)
            pool.wait_ge(s_ident0, 1)
            nc.gpsimd.affine_select(out=ident[:], in_=ident[:], compare_op=ALU.not_equal, fill=1.0, base=0,
                                    pattern=[[-1, P]], channel_multiplier=1).then_inc(s_ident, 1)

            def gather_block(b, par, reuse):
                pool.wait_ge(s_rows, b + 1)
                if reuse:
                    pool.wait_ge(s_trans, NT * (b - 1))
                pool.nop(nofuse=True)
                for k in range(GATHERS):
                    nc.gpsimd.indirect_dma_start(
                        gathered[:, par, k, :], None, table,
                        bass.IndirectOffsetOnAxis(rows[:, par, k:k + 1], 0)).then_inc(s_gather[par][k], 16)

            gather_block(0, 0, False)
            gather_block(1, 1, False)
            with pool.Fori(1, PAIRS) as i:
                gather_block(2 * i, 0, True)
                gather_block(2 * i + 1, 1, True)

        @block.scalar
        def _(act):
            def vectors(b, par, c, reuse):
                act.wait_ge(s_trans, NT * b + c + 1)
                for n, (row, s, ns, f, w) in enumerate(segments(*t_chunks[c])):
                    nc.scalar.copy(vecs[:, par, s:s + ns, 1 + f:1 + f + w],
                                   t_bank[c % 2][:, row:row + ns * w].rearrange("p (s f) -> p s f", f=w)
                                   ).then_inc(s_vecs, 1)

            def probability(b):
                act.wait_ge(s_top3_sum, b + 1)
                nc.scalar.activation(prob[:, bass.ds(b * BLOCK, BLOCK)], top3_bank[0:1, 0:BLOCK], ACT.Sigmoid,
                                     bias=tb3_sb[:, 0:1]).then_inc(s_prob, 1)

            def stage(b, par, first, reuse):
                if reuse:
                    act.wait_ge(s_top1_sum, b - 1)
                nc.scalar.copy(vecs[:, par, :, 0], bottom[:, bass.ds(b * BLOCK, BLOCK)]).then_inc(s_bot_in, 1)
                for c in range(NT):
                    if c == NT - 1 and not first:
                        probability(b - 1)
                    vectors(b, par, c, reuse)

            act.wait_ge(s_bottom, SAMPLES // SLICE)
            act.wait_ge(s_top, 16 * 6)
            stage(0, 0, True, False)
            stage(1, 1, False, False)
            with act.Fori(1, PAIRS) as i:
                stage(2 * i, 0, False, True)
                stage(2 * i + 1, 1, False, True)
            probability(BLOCKS - 1)

        seg_count = [len(segments(*ch)) for ch in t_chunks]
        SEGS = sum(seg_count)

        def segs_done(b, c):
            return SEGS * b + sum(seg_count[:c + 1])

        def prod_bank(par, m):
            return p_bank[m] if m < 3 else p_bank[m - 3]

        @block.vector
        def _(dve):
            def table_rows(b, par):
                idx = index_sb[:, bass.ds(b * GATHERS, GATHERS)]
                nc.vector.tensor_scalar(wrap[:, par, :], idx, 0.0, float(VOCAB), ALU.is_lt, ALU.mult).then_inc(s_wrap, 1)
                dve.wait_ge(s_wrap, b + 1)
                nc.vector.scalar_tensor_tensor(out=clipped[:, par, :], in0=idx, scalar=float(VOCAB - 1),
                                               in1=wrap[:, par, :], op0=ALU.min, op1=ALU.add).then_inc(s_clip, 1)
                dve.wait_ge(s_clip, b + 1)
                nc.vector.scalar_tensor_tensor(out=rows[:, par, :], in0=clipped[:, par, :], scalar=0.0,
                                               in1=base_sb[:], op0=ALU.max, op1=ALU.add).then_inc(s_rows, 1)

            def relu1(b, reuse):
                dve.wait_ge(s_top1_sum, b + 1)
                if reuse:
                    dve.wait_ge(s_top2_sum, b)
                nc.vector.tensor_scalar(top1[:], top1_bank[:, 0:BLOCK], tb1_sb[:, 0:1], 0.0,
                                        ALU.add, ALU.max).then_inc(s_top1, 1)

            def relu2(b, reuse):
                dve.wait_ge(s_top2_sum, b + 1)
                if reuse:
                    dve.wait_ge(s_top3_sum, b)
                nc.vector.tensor_scalar(top2[0:TOP2], top2_bank[0:TOP2, 0:BLOCK], tb2_sb[:, 0:1], 0.0,
                                        ALU.add, ALU.max).then_inc(s_top2, 1)

            def diagonal(b, par, m):
                _, g0, g1 = p_chunks[m]
                dve.wait_ge(s_prod, NP * b + m + 1)
                view = prod_bank(par, m)[:, 0:(g1 - g0) * PARTS * FIELDS].rearrange(
                    "p (q j g) -> p q j g", j=PARTS, g=FIELDS)
                for j in range(PARTS):
                    p0 = QUAD * j
                    nc.vector.tensor_copy(
                        dots[p0:p0 + FIELDS, par, :, PARTS * g0 + j:PARTS * (g1 - 1) + j + 1:PARTS].rearrange(
                            "p g q -> p q g"),
                        view[p0:p0 + FIELDS, :, j, :]).then_inc(s_dots, 1)

            def stage(b, par, first, second, last):
                if not first:
                    relu1(b - 1, not second)
                diagonal(b, par, 0)
                if not first:
                    relu2(b - 1, not second)
                for m in range(1, NP):
                    diagonal(b, par, m)
                if not last:
                    table_rows(b + 2, par)

            nc.vector.memset(dots[:], 0.0).then_inc(s_dots_zero, 1)
            nc.vector.memset(vecs[:, :, :, VECS:QUAD], 0.0).then_inc(s_pad_zero, 1)
            nc.vector.memset(top2[TOP2:], 0.0).then_inc(s_pad_zero, 1)
            nc.vector.memset(tw3_sb[TOP2:], 0.0).then_inc(s_pad_zero, 1)
            dve.wait_ge(s_index0, 32)
            table_rows(0, 0)
            table_rows(1, 1)
            nc.vector.memset(tw1_pair[:], 0.0).then_inc(s_pair_zero, 1)
            dve.wait_ge(s_xT, 16 * (4 + KH))
            for c in range(SAMPLES // SLICE):
                for k in range(KH):
                    dve.wait_ge(s_hid_sum, KH * c + k + 1)
                    if c:
                        dve.wait_ge(s_bot_sum, c)
                    nc.vector.tensor_scalar(hidden[:, k, :], t_bank[k % 2][:, :], bb1_sb[:, k:k + 1], 0.0,
                                            ALU.add, ALU.max).then_inc(s_hid, 1)
                dve.wait_ge(s_bot_sum, c + 1)
                nc.vector.tensor_scalar(bottom[:, c * SLICE:(c + 1) * SLICE], top1_bank[:, :], bb2_sb[:, 0:1], 0.0,
                                        ALU.add, ALU.max).then_inc(s_bottom, 1)
            dve.wait_ge(s_dots_zero, 1)
            dve.wait_ge(s_top, 16 * 6)
            dve.wait_ge(s_index, 16)
            stage(0, 0, True, False, False)
            stage(1, 1, False, True, False)
            with dve.Fori(1, PAIRS - 1) as i:
                stage(2 * i, 0, False, False, False)
                stage(2 * i + 1, 1, False, False, False)
            stage(BLOCKS - 2, 0, False, False, True)
            stage(BLOCKS - 1, 1, False, False, True)
            relu1(BLOCKS - 1, True)
            relu2(BLOCKS - 1, True)

        @block.tensor
        def _(pe):
            def bottom_mlp(c):
                cols = slice(c * SLICE, (c + 1) * SLICE)
                for k in range(KH):
                    if c:
                        pe.wait_ge(s_hid, KH * (c - 1) + k + 1)
                    nc.tensor.matmul(t_bank[k % 2][:, :], bw1_sb[:, k * P:(k + 1) * P], xT_sb[:, cols],
                                     start=True, stop=True).then_inc(s_hid_sum, 1)
                pe.wait_ge(s_hid, KH * (c + 1))
                if c:
                    pe.wait_ge(s_bottom, c)
                for k in range(KH):
                    last = nc.tensor.matmul(top1_bank[:, :], bw2_sb[:, k, :], hidden[:, k, :],
                                            start=(k == 0), stop=(k == KH - 1))
                last.then_inc(s_bot_sum, 1)

            def transposes(b, par, c, turn, first):
                if c >= 2:
                    pe.wait_ge(s_vecs, segs_done(b, c - 2))
                elif not first:
                    pe.wait_ge(s_vecs, segs_done(b - 1, c + NT - 2))
                k0, k1 = t_chunks[c]
                for k in range(k0, k1):
                    pe.wait_ge(s_gather[par][k], 16 * (turn + 1))
                    last = nc.tensor.transpose(t_bank[c % 2][:, (k - k0) * P:(k - k0 + 1) * P],
                                               gathered[:, par, k, :], ident[:])
                last.then_inc(s_trans, 1)

            def products(b, par, c, first):
                for m, (need, g0, g1) in enumerate(p_chunks):
                    if need != c:
                        continue
                    pe.wait_ge(s_vecs, segs_done(b, c))
                    if m == 0:
                        pe.wait_ge(s_bot_in, b + 1)
                    if m >= 3:
                        pe.wait_ge(s_dots, PARTS * (NP * b + m - 2))
                    elif not first:
                        pe.wait_ge(s_dots, PARTS * (NP * (b - 1) + (m + 3 if m + 3 < NP else m) + 1))
                    for g in range(g0, g1):
                        four = vecs[:, par, PARTS * g:PARTS * (g + 1), :]
                        cols = (g - g0) * PARTS * FIELDS
                        last = nc.tensor.matmul(prod_bank(par, m)[:, cols:cols + PARTS * FIELDS],
                                                four.rearrange("p j f -> p (j f)"), four[:, :, 1:VECS],
                                                start=True, stop=True)
                    last.then_inc(s_prod, 1)

            def layer1(b, par, first):
                pe.wait_ge(s_dots, PARTS * NP * (b + 1))
                if not first:
                    pe.wait_ge(s_top1, b)
                nc.tensor.matmul(top1_bank[:, 0:BLOCK], tw1_dense[:], vecs[:, par, :, 0], start=True, stop=False)
                for g in range(FIELDS):
                    last = nc.tensor.matmul(top1_bank[:, 0:BLOCK], tw1_pair[:, g, :], dots[:, par, g, :],
                                            start=False, stop=(g == FIELDS - 1))
                last.then_inc(s_top1_sum, 1)

            def layer2(b, first):
                pe.wait_ge(s_top1, b + 1)
                if not first:
                    pe.wait_ge(s_top2, b)
                nc.tensor.matmul(top2_bank[0:TOP2, 0:BLOCK], tw2_sb[:], top1[:],
                                 start=True, stop=True).then_inc(s_top2_sum, 1)

            def layer3(b, first):
                pe.wait_ge(s_top2, b + 1)
                if not first:
                    pe.wait_ge(s_prob, b)
                nc.tensor.matmul(top3_bank[0:1, 0:BLOCK], tw3_sb[:], top2[:],
                                 start=True, stop=True).then_inc(s_top3_sum, 1)

            def stage(b, par, turn, first, second):
                transposes(b, par, 0, turn, first)
                if not first:
                    layer1(b - 1, 1 - par, second)
                products(b, par, 0, first)
                transposes(b, par, 1, turn, first)
                if not first:
                    layer2(b - 1, second)
                products(b, par, 1, first)
                transposes(b, par, 2, turn, first)
                if not first:
                    layer3(b - 1, second)
                products(b, par, 2, first)
                for c in range(3, NT):
                    transposes(b, par, c, turn, first)
                    products(b, par, c, first)

            pe.wait_ge(s_xT, 16 * (4 + KH))
            for c in range(SAMPLES // SLICE):
                bottom_mlp(c)
            pe.wait_ge(s_ident, 1)
            pe.wait_ge(s_hid, KH * (SAMPLES // SLICE))
            pe.wait_ge(s_pad_zero, 3)
            pe.wait_ge(s_bottom, SAMPLES // SLICE)
            stage(0, 0, 0, True, False)
            pe.wait_ge(s_top, 16 * 6)
            pe.wait_ge(s_pair_copy, 16 * (PARTS - 1))
            pe.wait_ge(s_pair, 16 * FIELDS)
            stage(1, 1, 0, False, True)
            with pe.Fori(1, PAIRS) as i:
                stage(2 * i, 0, i, False, False)
                stage(2 * i + 1, 1, i, False, False)
            layer1(BLOCKS - 1, 1, False)
            layer2(BLOCKS - 1, False)
            layer3(BLOCKS - 1, False)


def kernel(r_dense_x, r_sparse_x, L0_rec_emb_tables, L0_rec_bw1, L0_rec_bb1, L0_rec_bw2, L0_rec_bb2,
           L0_rec_tw1, L0_rec_tb1, L0_rec_tw2, L0_rec_tb2, L0_rec_tw3, L0_rec_tb3):
    import numpy as np
    import concourse.bacc as bacc
    from concourse.bass_utils import run_bass_kernel_spmd

    samples, fields = r_sparse_x.shape
    vocab = L0_rec_emb_tables.shape[1]
    per_block = BLOCK * fields
    base = ((np.arange(per_block) % fields) * vocab).astype(np.int32).reshape(per_block // P, P).T
    ins = {
        "xT": np.ascontiguousarray(np.asarray(r_dense_x).T),
        "sparse": np.ascontiguousarray(np.asarray(r_sparse_x).reshape(samples * fields // P, P).T),
        "base": np.ascontiguousarray(base),
        "emb": L0_rec_emb_tables, "bw1": L0_rec_bw1, "bb1": L0_rec_bb1, "bw2": L0_rec_bw2, "bb2": L0_rec_bb2,
        "tw1": L0_rec_tw1, "tb1": L0_rec_tb1, "tw2": L0_rec_tw2, "tb2": L0_rec_tb2,
        "tw3": L0_rec_tw3, "tb3": L0_rec_tb3,
    }
    nc = bacc.Bacc("TRN2", target_bir_lowering=False, num_devices=1)
    arrays, args = {}, []
    for name, a in ins.items():
        a = np.ascontiguousarray(a)
        arrays[f"in_{name}"] = a
        args.append(nc.dram_tensor(f"in_{name}", a.shape, mybir.dt.from_np(a.dtype), kind="ExternalInput").ap())
    args.append(nc.dram_tensor("probabilities", (samples, 1), F32, kind="ExternalOutput").ap())
    dlrm_kernel(nc, *args)
    r = run_bass_kernel_spmd(nc, [arrays], core_ids=[0])
    return r.results[0]["probabilities"]
```

```python
from contextlib import ExitStack

import concourse.bass as bass
from concourse import mybir

F32 = mybir.dt.float32
I32 = mybir.dt.int32
U32 = mybir.dt.uint32
ALU = mybir.AluOpType
ACT = mybir.ActivationFunctionType

P = 128
BLOCK = 64
PAIR = 2 * BLOCK
PARTS = 4
QUAD = P // PARTS
T_BANK = 4


def dlrm_kernel(nc, xT, sparse, base, emb, bw1, bb1, bw2, bb2, tw1, tb1, tw2, tb2, tw3, tb3, out):
    DENSE, SAMPLES = xT.shape
    FIELDS, VOCAB, EMB = emb.shape
    HID = bw1.shape[1]
    KH = HID // P
    VECS = FIELDS + 1
    TOP1, TOP2 = tw2.shape
    BLOCKS = SAMPLES // BLOCK
    GATHERS = BLOCK * FIELDS // P
    GROUPS = BLOCK // PARTS
    PAIRS = BLOCKS // 2
    assert EMB == P and TOP1 == P and BLOCK * FIELDS == GATHERS * P and BLOCKS % 2 == 0 and HID == KH * P

    t_chunks = [(k, min(k + T_BANK, GATHERS)) for k in range(0, GATHERS, T_BANK)]
    NT = len(t_chunks)

    def segments(k0, k1):
        row, end, got = P * k0, P * k1, []
        while row < end:
            s, f = divmod(row, FIELDS)
            if f or end - row < FIELDS:
                n, w = 1, min(FIELDS - f, end - row)
            else:
                n, w = (end - row) // FIELDS, FIELDS
            got.append((row - P * k0, s, n, f, w))
            row += n * w
        return got

    groups_per_bank = 512 // (PARTS * FIELDS)
    p_chunks, at = [], 0
    for c, (_, k1) in enumerate(t_chunks):
        whole = P * k1 // FIELDS // PARTS
        if c < len(t_chunks) - 2:
            whole -= (whole - at) % groups_per_bank
        while at < whole:
            p_chunks.append((c, at, min(at + groups_per_bank, whole)))
            at = p_chunks[-1][2]
    assert at == GROUPS and len(p_chunks) == 5 and len(t_chunks) == 4
    NP = len(p_chunks)

    with ExitStack() as ctx:
        def sb(name, shape, dt=F32):
            return ctx.enter_context(nc.sbuf_tensor(name, shape, dt))

        def pb(name, shape):
            return ctx.enter_context(nc.psum_tensor(name, shape, F32))

        def sem(name):
            return ctx.enter_context(nc.semaphore(name))

        ident = sb("ident", [P, P])
        bw1_sb = sb("bw1_sb", [DENSE, HID])
        bw2_sb = sb("bw2_sb", [P, KH, EMB])
        bb1_sb = sb("bb1_sb", [P, KH])
        bb2_sb = sb("bb2_sb", [P, 1])
        tw1_dense = sb("tw1_dense", [P, TOP1])
        tw1_pair = sb("tw1_pair", [P, FIELDS, TOP1])
        tb1_sb = sb("tb1_sb", [P, 1])
        tw2_sb = sb("tw2_sb", [P, TOP2])
        tb2_sb = sb("tb2_sb", [TOP2, 1])
        tw3_sb = sb("tw3_sb", [P, 1])
        tb3_sb = sb("tb3_sb", [1, 1])
        base_sb = sb("base_sb", [P, GATHERS], I32)
        index_sb = sb("index_sb", [P, BLOCKS * GATHERS], I32)
        xT_sb = sb("xT_sb", [DENSE, SAMPLES])
        hidden = sb("hidden", [P, KH, PAIR])
        wrap = sb("wrap", [P, 2, GATHERS])
        clipped = sb("clipped", [P, 2, GATHERS])
        rows = sb("rows", [P, 2, GATHERS], U32)
        gathered = sb("gathered", [P, 2, GATHERS, EMB])
        vecs = sb("vecs", [P, 2, BLOCK, QUAD])
        dots = sb("dots", [P, FIELDS, PAIR])
        top1 = sb("top1", [P, PAIR])
        top2 = sb("top2", [P, PAIR])
        prob = sb("prob", [1, SAMPLES])

        t_bank = [pb(f"t_bank{i}", [P, 512]) for i in range(2)]
        p_bank = [pb(f"p_bank{i}", [P, 512]) for i in range(3)]
        top1_bank = pb("top1_bank", [P, 512])
        bottom_bank = pb("bottom_bank", [P, 512])
        top23_bank = pb("top23_bank", [P, 512])

        s_index0 = sem("s_index0")
        s_index = sem("s_index")
        s_xT = sem("s_xT")
        s_top = sem("s_top")
        s_pair = sem("s_pair")
        s_pair_copy = sem("s_pair_copy")
        s_pair_zero = sem("s_pair_zero")
        s_dots_zero = sem("s_dots_zero")
        s_pad_zero = sem("s_pad_zero")
        s_ident0 = sem("s_ident0")
        s_ident = sem("s_ident")
        s_hid_sum = sem("s_hid_sum")
        s_hid = sem("s_hid")
        s_bot_sum = sem("s_bot_sum")
        s_wrap = sem("s_wrap")
        s_clip = sem("s_clip")
        s_rows = sem("s_rows")
        s_gather = [[sem(f"s_gather{p}_{k}") for k in range(GATHERS)] for p in range(2)]
        s_trans = sem("s_trans")
        s_bottom = sem("s_bottom")
        s_vecs = sem("s_vecs")
        s_prod = sem("s_prod")
        s_dots = sem("s_dots")
        s_top1_sum = sem("s_top1_sum")
        s_top1 = sem("s_top1")
        s_top2_sum = sem("s_top2_sum")
        s_top2 = sem("s_top2")
        s_top3_sum = sem("s_top3_sum")
        s_prob = sem("s_prob")
        s_out = sem("s_out")

        table = emb.rearrange("f v d -> (f v) d")
        out_row = out.rearrange("(a s) o -> a (s o)", a=1)
        HEAD = 2 * GATHERS

        block = ctx.enter_context(nc.Block())

        @block.sync
        def _(sp):
            sp.dma_start(index_sb[:, 0:HEAD], sparse[:, 0:HEAD]).then_inc(s_index0, 16)
            sp.dma_start(base_sb[:], base).then_inc(s_index0, 16)
            sp.dma_start(xT_sb[:], xT).then_inc(s_xT, 16)
            sp.dma_start(bw1_sb[:], bw1).then_inc(s_xT, 16)
            for k in range(KH):
                sp.dma_start(bb1_sb[:, k:k + 1], bb1[k * P:(k + 1) * P].rearrange("(p a) -> p a", a=1)).then_inc(s_xT, 16)
            sp.dma_start(bw2_sb[:], bw2.rearrange("(k p) n -> p k n", p=P)).then_inc(s_xT, 16)
            sp.dma_start(bb2_sb[:], bb2.rearrange("(p a) -> p a", a=1)).then_inc(s_xT, 16)
            sp.dma_start(index_sb[:, HEAD:], sparse[:, HEAD:]).then_inc(s_index, 16)
            sp.wait_ge(s_pair_zero, 1)
            first = EMB
            for f in range(FIELDS):
                n = FIELDS - f
                sp.dma_start(tw1_pair[f:f + 1, f:FIELDS, :],
                             tw1[first:first + n, :].rearrange("(a g) n -> a g n", a=1)).then_inc(s_pair, 16)
                first += n
            sp.dma_start(tw1_dense[:], tw1[0:EMB, :]).then_inc(s_top, 16)
            sp.dma_start(tb1_sb[:], tb1.rearrange("(p a) -> p a", a=1)).then_inc(s_top, 16)
            sp.dma_start(tw2_sb[:], tw2).then_inc(s_top, 16)
            sp.dma_start(tb2_sb[:], tb2.rearrange("(p a) -> p a", a=1)).then_inc(s_top, 16)
            sp.dma_start(tw3_sb[0:TOP2], tw3).then_inc(s_top, 16)
            sp.dma_start(tb3_sb[:], tb3.rearrange("(p a) -> p a", a=1)).then_inc(s_top, 16)
            sp.wait_ge(s_pair, 16 * FIELDS)
            for q in range(1, PARTS):
                sp.dma_start(tw1_pair[QUAD * q:QUAD * q + FIELDS], tw1_pair[0:FIELDS]).then_inc(s_pair_copy, 16)
            most = SAMPLES - PAIR
            sp.wait_ge(s_prob, PAIRS - 1)
            sp.dma_start(out_row[:, 0:most], prob[:, 0:most]).then_inc(s_out, 16)
            sp.wait_ge(s_prob, PAIRS)
            sp.dma_start(out_row[:, most:], prob[:, most:]).then_inc(s_out, 16)
            sp.wait_ge(s_out, 32)

        @block.gpsimd
        def _(pool):
            nc.gpsimd.memset(tw1_pair[:], 0.0).then_inc(s_pair_zero, 1)
            nc.gpsimd.memset(ident[:], 0.0).then_inc(s_ident0, 1)
            pool.wait_ge(s_ident0, 1)
            nc.gpsimd.affine_select(out=ident[:], in_=ident[:], compare_op=ALU.not_equal, fill=1.0, base=0,
                                    pattern=[[-1, P]], channel_multiplier=1).then_inc(s_ident, 1)

            def gather_block(b, par, reuse):
                pool.wait_ge(s_rows, b + 1)
                if reuse:
                    pool.wait_ge(s_trans, NT * (b - 1))
                pool.nop(nofuse=True)
                for k in range(GATHERS):
                    nc.gpsimd.indirect_dma_start(
                        gathered[:, par, k, :], None, table,
                        bass.IndirectOffsetOnAxis(rows[:, par, k:k + 1], 0)).then_inc(s_gather[par][k], 16)

            gather_block(0, 0, False)
            gather_block(1, 1, False)
            with pool.Fori(1, PAIRS) as i:
                gather_block(2 * i, 0, True)
                gather_block(2 * i + 1, 1, True)

        @block.scalar
        def _(act):
            def vectors(b, par, c):
                act.wait_ge(s_trans, NT * b + c + 1)
                for row, s, ns, f, w in segments(*t_chunks[c]):
                    nc.scalar.copy(vecs[:, par, s:s + ns, 1 + f:1 + f + w],
                                   t_bank[c % 2][:, row:row + ns * w].rearrange("p (s f) -> p s f", f=w)
                                   ).then_inc(s_vecs, 1)

            def probability(i):
                act.wait_ge(s_top3_sum, i + 1)
                nc.scalar.activation(prob[:, bass.ds(i * PAIR, PAIR)], top23_bank[0:1, 0:PAIR], ACT.Sigmoid,
                                     bias=tb3_sb[:, 0:1]).then_inc(s_prob, 1)

            def pair(i, first):
                for par in range(2):
                    b = 2 * i + par
                    if not first:
                        act.wait_ge(s_prod, NP * (b - 1))
                    for c in range(NT):
                        if c == NT - 1 and par == 0 and not first:
                            probability(i - 1)
                        vectors(b, par, c)

            act.wait_ge(s_top, 16 * 6)
            pair(0, True)
            with act.Fori(1, PAIRS) as i:
                pair(i, False)
            probability(PAIRS - 1)

        seg_count = [len(segments(*ch)) for ch in t_chunks]
        SEGS = sum(seg_count)

        def segs_done(b, c):
            return SEGS * b + sum(seg_count[:c + 1])

        def same_bank_before(b, m):
            return NP * b + m - 2 if m >= 3 else NP * (b - 1) + (m + 4 if m + 3 < NP else m + 1)

        @block.vector
        def _(dve):
            def table_rows(b, par):
                idx = index_sb[:, bass.ds(b * GATHERS, GATHERS)]
                nc.vector.tensor_scalar(wrap[:, par, :], idx, 0.0, float(VOCAB), ALU.is_lt, ALU.mult).then_inc(s_wrap, 1)
                dve.wait_ge(s_wrap, b + 1)
                nc.vector.scalar_tensor_tensor(out=clipped[:, par, :], in0=idx, scalar=float(VOCAB - 1),
                                               in1=wrap[:, par, :], op0=ALU.min, op1=ALU.add).then_inc(s_clip, 1)
                dve.wait_ge(s_clip, b + 1)
                nc.vector.scalar_tensor_tensor(out=rows[:, par, :], in0=clipped[:, par, :], scalar=0.0,
                                               in1=base_sb[:], op0=ALU.max, op1=ALU.add).then_inc(s_rows, 1)

            def hidden_relu(i):
                dve.wait_ge(s_hid_sum, i + 1)
                for k in range(KH):
                    nc.vector.tensor_scalar(hidden[:, k, :], bottom_bank[:, k * PAIR:(k + 1) * PAIR],
                                            bb1_sb[:, k:k + 1], 0.0, ALU.add, ALU.max).then_inc(s_hid, 1)

            def bottom_relu(i):
                dve.wait_ge(s_bot_sum, i + 1)
                nc.vector.tensor_scalar(vecs[:, :, :, 0], bottom_bank[:, 0:PAIR].rearrange("p (a s) -> p a s", a=2),
                                        bb2_sb[:, 0:1], 0.0, ALU.add, ALU.max).then_inc(s_bottom, 1)

            def relu1(i):
                dve.wait_ge(s_top1_sum, i + 1)
                nc.vector.tensor_scalar(top1[:], top1_bank[:, 0:PAIR], tb1_sb[:, 0:1], 0.0,
                                        ALU.add, ALU.max).then_inc(s_top1, 1)

            def relu2(i):
                dve.wait_ge(s_top2_sum, i + 1)
                nc.vector.tensor_scalar(top2[0:TOP2], top23_bank[0:TOP2, 0:PAIR], tb2_sb[:, 0:1], 0.0,
                                        ALU.add, ALU.max).then_inc(s_top2, 1)

            def diagonal(b, par, m):
                _, g0, g1 = p_chunks[m]
                s0 = BLOCK * par + PARTS * g0
                dve.wait_ge(s_prod, NP * b + m + 1)
                view = p_bank[m % 3][:, 0:(g1 - g0) * PARTS * FIELDS].rearrange(
                    "p (q j g) -> p q j g", j=PARTS, g=FIELDS)
                for j in range(PARTS):
                    p0 = QUAD * j
                    nc.vector.tensor_copy(
                        dots[p0:p0 + FIELDS, :, s0 + j:s0 + PARTS * (g1 - g0 - 1) + j + 1:PARTS].rearrange(
                            "p g q -> p q g"),
                        view[p0:p0 + FIELDS, :, j, :]).then_inc(s_dots, 1)

            def pair(i, first=False, last=False):
                if not first:
                    relu1(i - 1)
                bottom_relu(i)
                for par in range(2):
                    b = 2 * i + par
                    diagonal(b, par, 0)
                    if par == 0 and not first:
                        relu2(i - 1)
                    if par == 1 and not last:
                        hidden_relu(i + 1)
                    for m in range(1, NP):
                        diagonal(b, par, m)
                    if not last:
                        table_rows(b + 2, par)

            dve.wait_ge(s_index0, 32)
            table_rows(0, 0)
            table_rows(1, 1)
            nc.vector.memset(vecs[:, :, :, VECS:QUAD], 0.0).then_inc(s_pad_zero, 1)
            nc.vector.memset(top2[TOP2:], 0.0).then_inc(s_pad_zero, 1)
            nc.vector.memset(tw3_sb[TOP2:], 0.0).then_inc(s_pad_zero, 1)
            dve.wait_ge(s_xT, 16 * (4 + KH))
            hidden_relu(0)
            nc.vector.memset(dots[:], 0.0).then_inc(s_dots_zero, 1)
            dve.wait_ge(s_dots_zero, 1)
            dve.wait_ge(s_top, 16 * 6)
            dve.wait_ge(s_index, 16)
            pair(0, first=True)
            with dve.Fori(1, PAIRS - 1) as i:
                pair(i)
            pair(PAIRS - 1, last=True)
            relu1(PAIRS - 1)
            relu2(PAIRS - 1)

        @block.tensor
        def _(pe):
            def hidden_layer(i):
                for k in range(KH):
                    last = nc.tensor.matmul(bottom_bank[:, k * PAIR:(k + 1) * PAIR], bw1_sb[:, k * P:(k + 1) * P],
                                            xT_sb[:, bass.ds(i * PAIR, PAIR)], start=True, stop=True)
                last.then_inc(s_hid_sum, 1)

            def bottom_layer(i):
                pe.wait_ge(s_hid, KH * (i + 1))
                for k in range(KH):
                    last = nc.tensor.matmul(bottom_bank[:, 0:PAIR], bw2_sb[:, k, :], hidden[:, k, :],
                                            start=(k == 0), stop=(k == KH - 1))
                last.then_inc(s_bot_sum, 1)

            def transposes(b, par, c, turn, first):
                if c >= 2:
                    pe.wait_ge(s_vecs, segs_done(b, c - 2))
                elif not first:
                    pe.wait_ge(s_vecs, segs_done(b - 1, c + NT - 2))
                k0, k1 = t_chunks[c]
                for k in range(k0, k1):
                    pe.wait_ge(s_gather[par][k], 16 * (turn + 1))
                    last = nc.tensor.transpose(t_bank[c % 2][:, (k - k0) * P:(k - k0 + 1) * P],
                                               gathered[:, par, k, :], ident[:])
                last.then_inc(s_trans, 1)

            def products(b, par, c, first):
                for m, (need, g0, g1) in enumerate(p_chunks):
                    if need != c:
                        continue
                    pe.wait_ge(s_vecs, segs_done(b, c))
                    if m == 0 and par == 0:
                        pe.wait_ge(s_bottom, b // 2 + 1)
                    if m >= 3 or not first:
                        pe.wait_ge(s_dots, PARTS * same_bank_before(b, m))
                    for g in range(g0, g1):
                        four = vecs[:, par, PARTS * g:PARTS * (g + 1), :]
                        cols = (g - g0) * PARTS * FIELDS
                        last = nc.tensor.matmul(p_bank[m % 3][:, cols:cols + PARTS * FIELDS],
                                                four.rearrange("p j f -> p (j f)"), four[:, :, 1:VECS],
                                                start=True, stop=True)
                    last.then_inc(s_prod, 1)

            def layer1(i, first):
                pe.wait_ge(s_dots, PARTS * NP * 2 * (i + 1))
                if not first:
                    pe.wait_ge(s_top1, i)
                nc.tensor.matmul(top1_bank[:, 0:PAIR], tw1_dense[:], vecs[:, :, :, 0], start=True, stop=False)
                for g in range(FIELDS):
                    last = nc.tensor.matmul(top1_bank[:, 0:PAIR], tw1_pair[:, g, :], dots[:, g, :],
                                            start=False, stop=(g == FIELDS - 1))
                last.then_inc(s_top1_sum, 1)

            def layer2(i, first):
                if not first:
                    pe.wait_ge(s_prob, i)
                pe.wait_ge(s_top1, i + 1)
                nc.tensor.matmul(top23_bank[0:TOP2, 0:PAIR], tw2_sb[:], top1[:],
                                 start=True, stop=True).then_inc(s_top2_sum, 1)

            def layer3(i):
                pe.wait_ge(s_top2, i + 1)
                nc.tensor.matmul(top23_bank[0:1, 0:PAIR], tw3_sb[:], top2[:],
                                 start=True, stop=True).then_inc(s_top3_sum, 1)

            def pair(i, first=False, second=False, last=False):
                for par in range(2):
                    b = 2 * i + par
                    fresh = first and par == 0
                    for c in range(NT):
                        transposes(b, par, c, i, fresh)
                        if par == 0 and c == 0:
                            if not first:
                                layer1(i - 1, second)
                            bottom_layer(i)
                        if par == 0 and c == 1 and not first:
                            layer2(i - 1, second)
                        if par == 0 and c == 2 and not first:
                            layer3(i - 1)
                        products(b, par, c, fresh)
                        if par == 1 and c == 0 and not last:
                            hidden_layer(i + 1)

            pe.wait_ge(s_xT, 16 * (4 + KH))
            hidden_layer(0)
            pe.wait_ge(s_ident, 1)
            pe.wait_ge(s_pad_zero, 3)
            pair(0, first=True)
            pe.wait_ge(s_top, 16 * 6)
            pe.wait_ge(s_pair_copy, 16 * (PARTS - 1))
            pe.wait_ge(s_pair, 16 * FIELDS)
            pair(1, second=True)
            with pe.Fori(2, PAIRS - 1) as i:
                pair(i)
            pair(PAIRS - 1, last=True)
            layer1(PAIRS - 1, False)
            layer2(PAIRS - 1, False)
            layer3(PAIRS - 1)


def kernel(r_dense_x, r_sparse_x, L0_rec_emb_tables, L0_rec_bw1, L0_rec_bb1, L0_rec_bw2, L0_rec_bb2,
           L0_rec_tw1, L0_rec_tb1, L0_rec_tw2, L0_rec_tb2, L0_rec_tw3, L0_rec_tb3):
    import numpy as np
    import concourse.bacc as bacc
    from concourse.bass_utils import run_bass_kernel_spmd

    samples, fields = r_sparse_x.shape
    vocab = L0_rec_emb_tables.shape[1]
    per_block = BLOCK * fields
    base = ((np.arange(per_block) % fields) * vocab).astype(np.int32).reshape(per_block // P, P).T
    ins = {
        "xT": np.ascontiguousarray(np.asarray(r_dense_x).T),
        "sparse": np.ascontiguousarray(np.asarray(r_sparse_x).reshape(samples * fields // P, P).T),
        "base": np.ascontiguousarray(base),
        "emb": L0_rec_emb_tables, "bw1": L0_rec_bw1, "bb1": L0_rec_bb1, "bw2": L0_rec_bw2, "bb2": L0_rec_bb2,
        "tw1": L0_rec_tw1, "tb1": L0_rec_tb1, "tw2": L0_rec_tw2, "tb2": L0_rec_tb2,
        "tw3": L0_rec_tw3, "tb3": L0_rec_tb3,
    }
    nc = bacc.Bacc("TRN2", target_bir_lowering=False, num_devices=1)
    arrays, args = {}, []
    for name, a in ins.items():
        a = np.ascontiguousarray(a)
        arrays[f"in_{name}"] = a
        args.append(nc.dram_tensor(f"in_{name}", a.shape, mybir.dt.from_np(a.dtype), kind="ExternalInput").ap())
    args.append(nc.dram_tensor("probabilities", (samples, 1), F32, kind="ExternalOutput").ap())
    dlrm_kernel(nc, *args)
    r = run_bass_kernel_spmd(nc, [arrays], core_ids=[0])
    return r.results[0]["probabilities"]
```

```python
from contextlib import ExitStack

import concourse.bass as bass
from concourse import mybir

F32 = mybir.dt.float32
I32 = mybir.dt.int32
U32 = mybir.dt.uint32
ALU = mybir.AluOpType
ACT = mybir.ActivationFunctionType

P = 128
BLOCK = 64
PAIR = 2 * BLOCK
QUADS = 4
QUAD = P // QUADS
BANK = 512


def dlrm_kernel(nc, xT, index, emb, bw1, bb1, bw2, bb2, tw1, tb1, tw2, tb2, tw3, tb3, out):
    DENSE, SAMPLES = xT.shape
    FIELDS, VOCAB, EMB = emb.shape
    HID = bw1.shape[1]
    KH = HID // P
    VECS = FIELDS + 1
    TOP1, TOP2 = tw2.shape
    BLOCKS = SAMPLES // BLOCK
    GATHERS = BLOCK * FIELDS // P
    PAIRS = BLOCKS // 2
    RUN = -(-FIELDS // QUADS)
    runs = [(RUN * q, min(RUN * (q + 1), FIELDS)) for q in range(QUADS)]
    assert EMB == P and TOP1 == P and BLOCK * FIELDS == GATHERS * P and BLOCKS % 2 == 0 and HID == KH * P

    t_chunks = [(k, min(k + BANK // P, GATHERS)) for k in range(0, GATHERS, BANK // P)]
    NT = len(t_chunks)

    def segments(k0, k1):
        row, end, got = P * k0, P * k1, []
        while row < end:
            s, f = divmod(row, FIELDS)
            if f or end - row < FIELDS:
                n, w = 1, min(FIELDS - f, end - row)
            else:
                n, w = (end - row) // FIELDS, FIELDS
            got.append((row - P * k0, s, n, f, w))
            row += n * w
        return got

    groups_per_bank = BANK // (QUADS * FIELDS)
    p_chunks, at = [], 0
    for c, (_, k1) in enumerate(t_chunks):
        whole = P * k1 // FIELDS // QUADS
        if c < len(t_chunks) - 2:
            whole -= (whole - at) % groups_per_bank
        while at < whole:
            p_chunks.append((c, at, min(at + groups_per_bank, whole)))
            at = p_chunks[-1][2]
    assert at * QUADS == BLOCK and len(p_chunks) == 5 and len(t_chunks) == 4
    NP = len(p_chunks)

    with ExitStack() as ctx:
        def sb(name, shape, dt=F32):
            return ctx.enter_context(nc.sbuf_tensor(name, shape, dt))

        def pb(name, shape):
            return ctx.enter_context(nc.psum_tensor(name, shape, F32))

        def sem(name):
            return ctx.enter_context(nc.semaphore(name))

        ident = sb("ident", [P, P])
        bw1_sb = sb("bw1_sb", [DENSE, HID])
        bw2_sb = sb("bw2_sb", [P, KH, EMB])
        bb1_sb = sb("bb1_sb", [P, KH])
        bb2_sb = sb("bb2_sb", [P, 1])
        tw1_dense = sb("tw1_dense", [P, TOP1])
        tw1_tri = sb("tw1_tri", [FIELDS, FIELDS, TOP1])
        tw1_pair = sb("tw1_pair", [P, RUN, TOP1])
        tb1_sb = sb("tb1_sb", [P, 1])
        tw2_sb = sb("tw2_sb", [P, TOP2])
        tb2_sb = sb("tb2_sb", [TOP2, 1])
        tw3_sb = sb("tw3_sb", [P, 1])
        tb3_sb = sb("tb3_sb", [1, 1])
        index_sb = sb("index_sb", [P, (1 + BLOCKS) * GATHERS], I32)
        xT_sb = sb("xT_sb", [DENSE, SAMPLES])
        hidden = sb("hidden", [P, KH, PAIR])
        wrap = sb("wrap", [P, 2, GATHERS])
        clipped = sb("clipped", [P, 2, GATHERS])
        rows = sb("rows", [P, 2, GATHERS], U32)
        gathered = sb("gathered", [P, 2, GATHERS, EMB])
        vecs = sb("vecs", [P, 2, BLOCK, QUAD])
        dots = sb("dots", [P, RUN, PAIR])
        top1 = sb("top1", [P, PAIR])
        top2 = sb("top2", [P, PAIR])
        prob = sb("prob", [1, SAMPLES])
        warm_up = sb("warm_up", [1, 1])

        t_bank = [pb(f"t_bank{i}", [P, BANK]) for i in range(2)]
        p_bank = [pb(f"p_bank{i}", [P, BANK]) for i in range(3)]
        top1_bank = pb("top1_bank", [P, BANK])
        bottom_bank = pb("bottom_bank", [P, BANK])
        top23_bank = pb("top23_bank", [P, BANK])

        s_index0 = sem("s_index0")
        s_index = sem("s_index")
        s_xT = sem("s_xT")
        s_top = sem("s_top")
        s_tri_zero = sem("s_tri_zero")
        s_tri = sem("s_tri")
        s_pair_zero = sem("s_pair_zero")
        s_pair = sem("s_pair")
        s_dots_zero = sem("s_dots_zero")
        s_pad_zero = sem("s_pad_zero")
        s_ident0 = sem("s_ident0")
        s_ident = sem("s_ident")
        s_hid_sum = sem("s_hid_sum")
        s_hid = sem("s_hid")
        s_bot_sum = sem("s_bot_sum")
        s_bottom = sem("s_bottom")
        s_wrap = sem("s_wrap")
        s_clip = sem("s_clip")
        s_rows = sem("s_rows")
        s_gather = [[sem(f"s_gather{p}_{k}") for k in range(GATHERS)] for p in range(2)]
        s_trans = sem("s_trans")
        s_vecs = sem("s_vecs")
        s_prod = sem("s_prod")
        s_dots_v = sem("s_dots_v")
        s_dots_a = sem("s_dots_a")
        s_top1_sum = sem("s_top1_sum")
        s_top1 = sem("s_top1")
        s_top2_sum = sem("s_top2_sum")
        s_top2 = sem("s_top2")
        s_top3_sum = sem("s_top3_sum")
        s_prob = sem("s_prob")
        s_warm_up = sem("s_warm_up")
        s_out = sem("s_out")

        table = emb.rearrange("f v d -> (f v) d")
        out_row = out.rearrange("(a s) o -> a (s o)", a=1)
        HEAD = (1 + 2) * GATHERS

        def same_bank_before(b, m):
            return NP * b + m - 2 if m >= 3 else NP * (b - 1) + (m + 4 if m + 3 < NP else m + 1)

        def pieces(par, m, samples):
            _, g0, g1 = p_chunks[m]
            s0, s1 = BLOCK * par + QUADS * g0, BLOCK * par + QUADS * (g1 - 1) + 1
            view = p_bank[m % 3][:, 0:(g1 - g0) * QUADS * FIELDS].rearrange("p (q j g) -> p q j g", j=QUADS, g=FIELDS)
            for j in samples:
                for q, (lo, hi) in enumerate(runs):
                    yield (dots[QUAD * q:QUAD * q + FIELDS, 0:hi - lo, s0 + j:s1 + j:QUADS].rearrange("p g q -> p q g"),
                           view[QUAD * j:QUAD * j + FIELDS, :, j, lo:hi])

        block = ctx.enter_context(nc.Block())

        @block.sync
        def _(sp):
            sp.dma_start(index_sb[:, 0:HEAD], index[:, 0:HEAD]).then_inc(s_index0, 16)
            sp.dma_start(xT_sb[:], xT).then_inc(s_xT, 16)
            sp.dma_start(bw1_sb[:], bw1).then_inc(s_xT, 16)
            for k in range(KH):
                sp.dma_start(bb1_sb[:, k:k + 1], bb1[k * P:(k + 1) * P].rearrange("(p a) -> p a", a=1)).then_inc(s_xT, 16)
            sp.dma_start(bw2_sb[:], bw2.rearrange("(k p) n -> p k n", p=P)).then_inc(s_xT, 16)
            sp.dma_start(bb2_sb[:], bb2.rearrange("(p a) -> p a", a=1)).then_inc(s_xT, 16)
            sp.dma_start(index_sb[:, HEAD:], index[:, HEAD:]).then_inc(s_index, 16)
            sp.dma_start(tw1_dense[:], tw1[0:EMB, :]).then_inc(s_top, 16)
            sp.dma_start(tb1_sb[:], tb1.rearrange("(p a) -> p a", a=1)).then_inc(s_top, 16)
            sp.dma_start(tw2_sb[:], tw2).then_inc(s_top, 16)
            sp.dma_start(tb2_sb[:], tb2.rearrange("(p a) -> p a", a=1)).then_inc(s_top, 16)
            sp.dma_start(tw3_sb[0:TOP2], tw3).then_inc(s_top, 16)
            sp.dma_start(tb3_sb[:], tb3.rearrange("(p a) -> p a", a=1)).then_inc(s_top, 16)
            sp.wait_ge(s_tri_zero, 1)
            first = EMB
            for f in range(FIELDS):
                n = FIELDS - f
                sp.dma_start(tw1_tri[f:f + 1, f:FIELDS, :],
                             tw1[first:first + n, :].rearrange("(a g) n -> a g n", a=1)).then_inc(s_tri, 16)
                first += n
            sp.wait_ge(s_tri, 16 * FIELDS)
            sp.wait_ge(s_pair_zero, 1)
            for q in range(QUADS):
                g0, g1 = runs[q]
                sp.dma_start(tw1_pair[QUAD * q:QUAD * q + FIELDS, 0:g1 - g0, :],
                             tw1_tri[:, g0:g1, :]).then_inc(s_pair, 16)
            most = SAMPLES - PAIR
            sp.wait_ge(s_prob, PAIRS - 1)
            sp.dma_start(out_row[:, 0:most], prob[:, 0:most]).then_inc(s_out, 16)
            sp.wait_ge(s_prob, PAIRS)
            sp.dma_start(out_row[:, most:], prob[:, most:]).then_inc(s_out, 16)
            sp.wait_ge(s_out, 32)

        @block.gpsimd
        def _(pool):
            nc.gpsimd.memset(tw1_tri[:], 0.0).then_inc(s_tri_zero, 1)
            nc.gpsimd.memset(ident[:], 0.0).then_inc(s_ident0, 1)
            pool.wait_ge(s_ident0, 1)
            nc.gpsimd.affine_select(out=ident[:], in_=ident[:], compare_op=ALU.not_equal, fill=1.0, base=0,
                                    pattern=[[-1, P]], channel_multiplier=1).then_inc(s_ident, 1)

            def gather_block(b, par, reuse):
                pool.wait_ge(s_rows, b + 1)
                if reuse:
                    pool.wait_ge(s_trans, NT * (b - 1))
                pool.nop(nofuse=True)
                for k in range(GATHERS):
                    nc.gpsimd.indirect_dma_start(
                        gathered[:, par, k, :], None, table,
                        bass.IndirectOffsetOnAxis(rows[:, par, k:k + 1], 0)).then_inc(s_gather[par][k], 16)

            gather_block(0, 0, False)
            gather_block(1, 1, False)
            with pool.Fori(1, PAIRS) as i:
                gather_block(2 * i, 0, True)
                gather_block(2 * i + 1, 1, True)

        @block.scalar
        def _(act):
            def vectors(b, par, c):
                act.wait_ge(s_trans, NT * b + c + 1)
                for row, s, ns, f, w in segments(*t_chunks[c]):
                    last = nc.scalar.copy(vecs[:, par, s:s + ns, 1 + f:1 + f + w],
                                          t_bank[c % 2][:, row:row + ns * w].rearrange("p (s f) -> p s f", f=w))
                last.then_inc(s_vecs, 1)

            def products_kept(b, par, m):
                act.wait_ge(s_prod, NP * b + m + 1)
                for to, at in pieces(par, m, range(QUADS // 2, QUADS)):
                    last = nc.scalar.copy(to, at)
                last.then_inc(s_dots_a, 1)

            def probability(i):
                act.wait_ge(s_top3_sum, i + 1)
                nc.scalar.activation(prob[:, bass.ds(i * PAIR, PAIR)], top23_bank[0:1, 0:PAIR], ACT.Sigmoid,
                                     bias=tb3_sb[:, 0:1]).then_inc(s_prob, 1)

            def pair(i, first=False, last=False):
                if not first:
                    act.wait_ge(s_prod, NP * (2 * i - 1))
                vectors(2 * i, 0, 0)
                if not first:
                    products_kept(2 * i - 1, 1, 3)
                    products_kept(2 * i - 1, 1, 4)
                vectors(2 * i, 0, 1)
                vectors(2 * i, 0, 2)
                products_kept(2 * i, 0, 0)
                products_kept(2 * i, 0, 1)
                vectors(2 * i, 0, 3)
                if not first:
                    probability(i - 1)
                products_kept(2 * i, 0, 2)
                if not first:
                    act.wait_ge(s_prod, NP * (2 * i))
                vectors(2 * i + 1, 1, 0)
                products_kept(2 * i, 0, 3)
                products_kept(2 * i, 0, 4)
                if last:
                    products_kept(2 * i + 1, 1, 0)
                    for c in range(1, NT):
                        vectors(2 * i + 1, 1, c)
                        products_kept(2 * i + 1, 1, c)
                    products_kept(2 * i + 1, 1, 4)
                else:
                    for c in range(1, NT):
                        vectors(2 * i + 1, 1, c)
                        products_kept(2 * i + 1, 1, c - 1)

            act.wait_ge(s_dots_zero, 1)
            act.wait_ge(s_ident, 1)
            nc.scalar.activation(warm_up[:], ident[0:1, 0:1], ACT.Sigmoid).then_inc(s_warm_up, 1)
            act.wait_ge(s_warm_up, 1)
            pair(0, first=True)
            act.wait_ge(s_top, 16 * 6)
            with act.Fori(1, PAIRS - 1) as i:
                pair(i)
            pair(PAIRS - 1, last=True)
            probability(PAIRS - 1)

        @block.vector
        def _(dve):
            def table_rows(b, par):
                idx = index_sb[:, bass.ds((b + 1) * GATHERS, GATHERS)]
                nc.vector.tensor_scalar(wrap[:, par, :], idx, 0.0, float(VOCAB), ALU.is_lt, ALU.mult).then_inc(s_wrap, 1)
                dve.wait_ge(s_wrap, b + 1)
                nc.vector.scalar_tensor_tensor(out=clipped[:, par, :], in0=idx, scalar=float(VOCAB - 1),
                                               in1=wrap[:, par, :], op0=ALU.min, op1=ALU.add).then_inc(s_clip, 1)
                dve.wait_ge(s_clip, b + 1)
                nc.vector.scalar_tensor_tensor(out=rows[:, par, :], in0=clipped[:, par, :], scalar=0.0,
                                               in1=index_sb[:, 0:GATHERS], op0=ALU.max, op1=ALU.add).then_inc(s_rows, 1)

            def hidden_relu(i):
                dve.wait_ge(s_hid_sum, i + 1)
                for k in range(KH):
                    nc.vector.tensor_scalar(hidden[:, k, :], bottom_bank[:, k * PAIR:(k + 1) * PAIR],
                                            bb1_sb[:, k:k + 1], 0.0, ALU.add, ALU.max).then_inc(s_hid, 1)

            def bottom_relu(i):
                dve.wait_ge(s_bot_sum, i + 1)
                nc.vector.tensor_scalar(vecs[:, :, :, 0], bottom_bank[:, 0:PAIR].rearrange("p (a s) -> p a s", a=2),
                                        bb2_sb[:, 0:1], 0.0, ALU.add, ALU.max).then_inc(s_bottom, 1)

            def relu1(i):
                dve.wait_ge(s_top1_sum, i + 1)
                nc.vector.tensor_scalar(top1[:], top1_bank[:, 0:PAIR], tb1_sb[:, 0:1], 0.0,
                                        ALU.add, ALU.max).then_inc(s_top1, 1)

            def relu2(i):
                dve.wait_ge(s_top2_sum, i + 1)
                nc.vector.tensor_scalar(top2[0:TOP2], top23_bank[0:TOP2, 0:PAIR], tb2_sb[:, 0:1], 0.0,
                                        ALU.add, ALU.max).then_inc(s_top2, 1)

            def products_kept(b, par, m):
                dve.wait_ge(s_prod, NP * b + m + 1)
                for to, at in pieces(par, m, range(QUADS // 2)):
                    last = nc.vector.tensor_copy(to, at)
                last.then_inc(s_dots_v, 1)

            def pair(i, first=False, last=False):
                if not first:
                    products_kept(2 * i - 1, 1, 3)
                    products_kept(2 * i - 1, 1, 4)
                    relu1(i - 1)
                bottom_relu(i)
                if not first:
                    relu2(i - 1)
                for m in range(3):
                    products_kept(2 * i, 0, m)
                if not last:
                    table_rows(2 * i + 2, 0)
                products_kept(2 * i, 0, 3)
                products_kept(2 * i, 0, 4)
                if not last:
                    hidden_relu(i + 1)
                for m in range(NP if last else 3):
                    products_kept(2 * i + 1, 1, m)
                if not last:
                    table_rows(2 * i + 3, 1)

            dve.wait_ge(s_index0, 16)
            table_rows(0, 0)
            table_rows(1, 1)
            nc.vector.memset(vecs[:, :, :, VECS:QUAD], 0.0).then_inc(s_pad_zero, 1)
            nc.vector.memset(top2[TOP2:], 0.0).then_inc(s_pad_zero, 1)
            nc.vector.memset(tw3_sb[TOP2:], 0.0).then_inc(s_pad_zero, 1)
            dve.wait_ge(s_xT, 16 * (4 + KH))
            hidden_relu(0)
            nc.vector.memset(dots[:], 0.0).then_inc(s_dots_zero, 1)
            nc.vector.memset(tw1_pair[:], 0.0).then_inc(s_pair_zero, 1)
            dve.wait_ge(s_dots_zero, 1)
            dve.wait_ge(s_index, 16)
            dve.wait_ge(s_top, 16 * 6)
            pair(0, first=True)
            with dve.Fori(1, PAIRS - 1) as i:
                pair(i)
            pair(PAIRS - 1, last=True)
            relu1(PAIRS - 1)
            relu2(PAIRS - 1)

        @block.tensor
        def _(pe):
            def hidden_layer(i):
                for k in range(KH):
                    last = nc.tensor.matmul(bottom_bank[:, k * PAIR:(k + 1) * PAIR], bw1_sb[:, k * P:(k + 1) * P],
                                            xT_sb[:, bass.ds(i * PAIR, PAIR)], start=True, stop=True)
                last.then_inc(s_hid_sum, 1)

            def bottom_layer(i):
                pe.wait_ge(s_hid, KH * (i + 1))
                for k in range(KH):
                    last = nc.tensor.matmul(bottom_bank[:, 0:PAIR], bw2_sb[:, k, :], hidden[:, k, :],
                                            start=(k == 0), stop=(k == KH - 1))
                last.then_inc(s_bot_sum, 1)

            def transposes(b, par, c, turn, first):
                if c >= 2:
                    pe.wait_ge(s_vecs, NT * b + c - 1)
                elif not first:
                    pe.wait_ge(s_vecs, NT * (b - 1) + c + NT - 1)
                k0, k1 = t_chunks[c]
                for k in range(k0, k1):
                    pe.wait_ge(s_gather[par][k], 16 * (turn + 1))
                    last = nc.tensor.transpose(t_bank[c % 2][:, (k - k0) * P:(k - k0 + 1) * P],
                                               gathered[:, par, k, :], ident[:])
                last.then_inc(s_trans, 1)

            def products(b, par, m, first):
                need, g0, g1 = p_chunks[m]
                pe.wait_ge(s_vecs, NT * b + need + 1)
                if m == 0 and par == 0:
                    pe.wait_ge(s_bottom, b // 2 + 1)
                if m >= 3 or not first:
                    pe.wait_ge(s_dots_v, same_bank_before(b, m))
                    pe.wait_ge(s_dots_a, same_bank_before(b, m))
                for g in range(g0, g1):
                    four = vecs[:, par, QUADS * g:QUADS * (g + 1), :]
                    cols = (g - g0) * QUADS * FIELDS
                    last = nc.tensor.matmul(p_bank[m % 3][:, cols:cols + QUADS * FIELDS],
                                            four.rearrange("p j f -> p (j f)"), four[:, :, 1:VECS],
                                            start=True, stop=True)
                last.then_inc(s_prod, 1)

            def layer1(i, first):
                if not first:
                    pe.wait_ge(s_top1, i)
                nc.tensor.matmul(top1_bank[:, 0:PAIR], tw1_dense[:], vecs[:, :, :, 0], start=True, stop=False)
                pe.wait_ge(s_dots_v, NP * 2 * (i + 1))
                pe.wait_ge(s_dots_a, NP * 2 * (i + 1))
                for g in range(RUN):
                    last = nc.tensor.matmul(top1_bank[:, 0:PAIR], tw1_pair[:, g, :], dots[:, g, :],
                                            start=False, stop=(g == RUN - 1))
                last.then_inc(s_top1_sum, 1)

            def layer2(i, first):
                if not first:
                    pe.wait_ge(s_prob, i)
                pe.wait_ge(s_top1, i + 1)
                nc.tensor.matmul(top23_bank[0:TOP2, 0:PAIR], tw2_sb[:], top1[:],
                                 start=True, stop=True).then_inc(s_top2_sum, 1)

            def layer3(i):
                pe.wait_ge(s_top2, i + 1)
                nc.tensor.matmul(top23_bank[0:1, 0:PAIR], tw3_sb[:], top2[:],
                                 start=True, stop=True).then_inc(s_top3_sum, 1)

            def pair(i, first=False, second=False, last=False):
                transposes(2 * i, 0, 0, i, first)
                if not first:
                    products(2 * i - 1, 1, 3, first)
                    products(2 * i - 1, 1, 4, first)
                transposes(2 * i, 0, 1, i, first)
                if not first:
                    layer1(i - 1, second)
                bottom_layer(i)
                transposes(2 * i, 0, 2, i, first)
                if not first:
                    layer2(i - 1, second)
                products(2 * i, 0, 0, first)
                products(2 * i, 0, 1, first)
                transposes(2 * i, 0, 3, i, first)
                if not first:
                    layer3(i - 1)
                products(2 * i, 0, 2, first)
                transposes(2 * i + 1, 1, 0, i, False)
                products(2 * i, 0, 3, first)
                products(2 * i, 0, 4, first)
                if not last:
                    hidden_layer(i + 1)
                if last:
                    products(2 * i + 1, 1, 0, False)
                    for c in range(1, NT):
                        transposes(2 * i + 1, 1, c, i, False)
                        products(2 * i + 1, 1, c, False)
                    products(2 * i + 1, 1, 4, False)
                else:
                    for c in range(1, NT):
                        transposes(2 * i + 1, 1, c, i, False)
                        products(2 * i + 1, 1, c - 1, False)

            pe.wait_ge(s_xT, 16 * (4 + KH))
            hidden_layer(0)
            pe.wait_ge(s_ident, 1)
            pe.wait_ge(s_pad_zero, 3)
            pair(0, first=True)
            pe.wait_ge(s_top, 16 * 6)
            pe.wait_ge(s_pair, 16 * QUADS)
            pair(1, second=True)
            with pe.Fori(2, PAIRS - 1) as i:
                pair(i)
            pair(PAIRS - 1, last=True)
            layer1(PAIRS - 1, False)
            layer2(PAIRS - 1, False)
            layer3(PAIRS - 1)


def kernel(r_dense_x, r_sparse_x, L0_rec_emb_tables, L0_rec_bw1, L0_rec_bb1, L0_rec_bw2, L0_rec_bb2,
           L0_rec_tw1, L0_rec_tb1, L0_rec_tw2, L0_rec_tb2, L0_rec_tw3, L0_rec_tb3):
    import numpy as np
    import concourse.bacc as bacc
    from concourse.bass_utils import run_bass_kernel_spmd

    samples, fields = r_sparse_x.shape
    vocab = L0_rec_emb_tables.shape[1]
    per_block = BLOCK * fields
    base = ((np.arange(per_block) % fields) * vocab).astype(np.int32).reshape(per_block // P, P).T
    ins = {
        "xT": np.ascontiguousarray(np.asarray(r_dense_x).T),
        "index": np.concatenate([base, np.asarray(r_sparse_x).reshape(samples * fields // P, P).T], axis=1),
        "emb": L0_rec_emb_tables, "bw1": L0_rec_bw1, "bb1": L0_rec_bb1, "bw2": L0_rec_bw2, "bb2": L0_rec_bb2,
        "tw1": L0_rec_tw1, "tb1": L0_rec_tb1, "tw2": L0_rec_tw2, "tb2": L0_rec_tb2,
        "tw3": L0_rec_tw3, "tb3": L0_rec_tb3,
    }
    nc = bacc.Bacc("TRN2", target_bir_lowering=False, num_devices=1)
    arrays, args = {}, []
    for name, a in ins.items():
        a = np.ascontiguousarray(a)
        arrays[f"in_{name}"] = a
        args.append(nc.dram_tensor(f"in_{name}", a.shape, mybir.dt.from_np(a.dtype), kind="ExternalInput").ap())
    args.append(nc.dram_tensor("probabilities", (samples, 1), F32, kind="ExternalOutput").ap())
    dlrm_kernel(nc, *args)
    r = run_bass_kernel_spmd(nc, [arrays], core_ids=[0])
    return r.results[0]["probabilities"]
```
